# Optimizing a Trainium2 kernel written in Bass

```python
import numpy as np
import jax
import jax.numpy as jnp

def _softmax(x, axis=-1):
    return jax.nn.softmax(x, axis=axis)

def _gelu(x):
    return jax.nn.gelu(x, approximate=True)

def _silu(x):
    return jax.nn.silu(x)

def _sigmoid(x):
    return jax.nn.sigmoid(x)

def _layernorm(x, axis=-1, eps=1e-05):
    m = jnp.mean(x, axis=axis, keepdims=True)
    v = jnp.var(x, axis=axis, keepdims=True)
    return (x - m) / jnp.sqrt(v + eps)

def _scatter_add(tgt, idx, src, axis=0):
    return tgt.at[idx].add(src)

def _segment_sum(src, seg, n):
    return jax.ops.segment_sum(src, seg, n)
kernel_name = 'mk_cond_resid_d2_seqx_r4_0ffcd6'

def setup_inputs(seed: int=0):
    np.random.seed(seed)
    _w = jnp.asarray

    def _rec_inputs():
        import jax
        import jax.numpy as jnp
        _rk = jax.random.key(seed)
        x = -0.000125 + 0.9999 * jax.random.normal(jax.random.fold_in(_rk, 1), (128, 64, 1024), jnp.float32)
        _lenS = 64 - jax.random.randint(jax.random.fold_in(_rk, 7), (128,), 0, max(1, 64 // 4) + 1, jnp.int32)
        _lenS2 = 64 - jax.random.randint(jax.random.fold_in(_rk, 8), (128,), 0, max(1, 64 // 4) + 1, jnp.int32)
        itok_B_3_7 = jax.random.randint(jax.random.fold_in(_rk, 11), (128,), 3, 8, jnp.int32)
        itok_B_0_15 = jax.random.randint(jax.random.fold_in(_rk, 12), (128,), 0, 16, jnp.int32)
        return (x, itok_B_3_7, itok_B_0_15)
    x, itok_B_3_7, itok_B_0_15 = _rec_inputs()

    def _L0_cond_setup():
        import jax, jax.numpy as jnp
        import numpy as np
        RANK = 16
        ALPHA = 16.0
        SCALING = ALPHA / RANK
        N_ADAPTERS = 8
        IN_F = 1024
        OUT_F = 1024
        BATCH = 4
        SEQ = 512
        key = jax.random.key(seed)
        kx, ka, kb, ki = jax.random.split(key, 4)
        x = jax.random.normal(kx, (BATCH, SEQ, IN_F), dtype=jnp.float32)
        A = jax.random.normal(ka, (N_ADAPTERS, OUT_F, RANK), dtype=jnp.float32) * 0.02
        B = jax.random.normal(kb, (N_ADAPTERS, RANK, IN_F), dtype=jnp.float32) * 0.02
        adapter_ids = jax.random.randint(ki, (BATCH,), 0, N_ADAPTERS, dtype=jnp.int32)
        return {'x': x, 'A': A, 'B': B, 'adapter_ids': adapter_ids}
    _L0_cond_all = _L0_cond_setup()
    _L0_cond_in = {k: v for k, v in _L0_cond_all.items() if k in ('A', 'B')}
    del _L0_cond_all

    def _L1_cond_setup():
        import jax, jax.numpy as jnp
        import numpy as np
        NUM_CONDITIONS = 16
        IN_CH = 64
        OUT_CH = 64
        B = 64
        T = 1024
        key = jax.random.key(seed)
        k_x, k_w, k_c = jax.random.split(key, 3)
        x = jax.random.normal(k_x, (B, IN_CH, T), dtype=jnp.float32)
        bound = float(np.sqrt(6.0 / IN_CH))
        weights = jax.random.uniform(k_w, (NUM_CONDITIONS, IN_CH, OUT_CH), dtype=jnp.float32, minval=-bound, maxval=bound)
        condition = jax.random.randint(k_c, (B,), 0, NUM_CONDITIONS, dtype=jnp.int64)
        return {'x': x, 'weights': weights, 'condition': condition}
    _L1_cond_all = _L1_cond_setup()
    _L1_cond_in = {k: v for k, v in _L1_cond_all.items() if k in ('weights',)}
    del _L1_cond_all
    return {'x': x, 'itok_B_3_7': itok_B_3_7, 'itok_B_0_15': itok_B_0_15, 'L0_cond_A': _L0_cond_in['A'], 'L0_cond_B': _L0_cond_in['B'], 'L1_cond_weights': _L1_cond_in['weights']}

def reference(x, itok_B_3_7, itok_B_0_15, L0_cond_A, L0_cond_B, L1_cond_weights):
    import jax
    import jax.numpy as jnp

    def _L0_cond_ref(x, A, B, adapter_ids):
        import jax, jax.numpy as jnp
        import numpy as np
        RANK = 16
        ALPHA = 16.0
        SCALING = ALPHA / RANK
        N_ADAPTERS = 8
        IN_F = 1024
        OUT_F = 1024
        BATCH = 4
        SEQ = 512
        B_sel = B[adapter_ids]
        A_sel = A[adapter_ids]
        Bx = jnp.einsum('bni,bri->bnr', x, B_sel)
        out = jnp.einsum('bnr,bor->bno', Bx, A_sel)
        return out * SCALING

    def _L1_cond_ref(x, weights, condition):
        import jax, jax.numpy as jnp
        import numpy as np
        NUM_CONDITIONS = 16
        IN_CH = 64
        OUT_CH = 64
        B = 64
        T = 1024
        W = weights[condition]
        return jnp.einsum('bct,bcd->bdt', x, W)
    x = x + _L0_cond_ref(x, L0_cond_A, L0_cond_B, itok_B_3_7)
    x = x + _L1_cond_ref(x, L1_cond_weights, itok_B_0_15)
    return x

_drawn_inputs = setup_inputs


def setup_inputs(seed=0):
    import zlib

    import numpy as np

    out = dict(_drawn_inputs(seed))
    spreads = {}
    factors = {}
    for name, (base, spread) in spreads.items():
        noise = np.random.default_rng([zlib.crc32(name.encode()), seed]).standard_normal(out[name].shape)
        drawn = base * np.exp(spread * noise) if base else spread * noise
        out[name] = jnp.asarray(drawn.astype(out[name].dtype))
    for name, factor in factors.items():
        out[name] = (out[name] * factor).astype(out[name].dtype)
    return out
```

```python
from contextlib import ExitStack

import concourse.bass as bass
from concourse import mybir

ALU = mybir.AluOpType
F32 = mybir.dt.float32
F32R = mybir.dt.float32r
I32 = mybir.dt.int32

P = 128
PAIR = 2
RING = 4
BANK = 512
SLOTS = 4
TILE_COLS = 32


def cond_resid_kernel(nc, x, adapter_id, mix_id, lora_a, lora_b, mix_w, ident, pair_mask, spread, low_rows, slot_part,
                      chunk_rows, out):
    batches, C, T = x.shape
    adapters, _, R = lora_a.shape
    mixes = mix_w.shape[0]
    pairs = batches // PAIR
    K = T // P
    H = T // BANK
    KH = K // H
    AH = adapters // H
    PART = P // PAIR
    assert C == PART and adapters * R == P and PAIR * SLOTS * R == P and PAIR * R == TILE_COLS
    assert pairs % RING == 0 and H == 2

    x_dram = x.rearrange("(n b) c t -> n (b c) t", b=PAIR)
    out_dram = out.rearrange("(n b) c t -> n (b c) t", b=PAIR)

    with ExitStack() as ctx:
        def sb(name, shape, dt=F32):
            return ctx.enter_context(nc.sbuf_tensor(name, shape, dt))

        def psum(name, shape):
            return ctx.enter_context(nc.psum_tensor(name, shape, F32))

        def sem(name):
            return ctx.enter_context(nc.semaphore(name))

        ids = sb("ids", [1, 2, batches], I32)
        identity = sb("identity", [P, P])
        pair_diag = sb("pair_diag", [P, P])
        spread_sb = sb("spread_sb", [P, P])
        low_sb = sb("low_sb", [P, 1])
        slot_sb = sb("slot_sb", [P, 2, P])
        chunk_sb = sb("chunk_sb", [P, K])
        pick_chunk = sb("pick_chunk", [P, K, 2, P], F32R)
        a_turned = sb("a_turned", [P, 2, T], F32R)
        a_rows = sb("a_rows", [P, adapters, K, R])
        b_rows = sb("b_rows", [P, T])
        b_table = sb("b_table", [P, K, adapters, R])
        a_table = sb("a_table", [P, adapters, T], F32R)
        w_full = sb("w_full", [P, mixes, C])
        w_parts = sb("w_parts", [P, mixes, 2, C], F32R)

        x_sb = sb("x_sb", [P, RING, T])
        x_hi = sb("x_hi", [P, RING, T], F32R)
        x_lo = sb("x_lo", [P, RING, T], F32R)
        x_t = sb("x_t", [P, 2, K, P])
        b_pair = sb("b_pair", [P, 2, K, PAIR, R])
        w_pair = sb("w_pair", [P, 2, P])
        w_pair_parts = sb("w_pair_parts", [P, 2, 2, P], F32R)
        a_pair = sb("a_pair", [P, 2, T], F32R)
        bx_t = sb("bx_t", [P, P])
        bx = sb("bx", [P, P])
        v_hi = sb("v_hi", [P, P], F32R)
        v_pair = sb("v_pair", [P, 2, P], F32R)
        y_sb = sb("y_sb", [P, RING, T])

        ps_xt = psum("ps_xt", [P, 2, BANK])
        ps_out = psum("ps_out", [P, 2, H, BANK])
        ps_bx = psum("ps_bx", [P, BANK])
        ps_sv = psum("ps_sv", [P, 2, P])
        ps_s, ps_v = ps_sv[:, 0, :], ps_sv[:, 1, :]

        consts_loaded = sem("consts_loaded")
        a_loaded = sem("a_loaded")
        b_loaded = sem("b_loaded")
        w_loaded = sem("w_loaded")
        zeroed = sem("zeroed")
        bt_turned = sem("bt_turned")
        bt_copied = sem("bt_copied")
        chunks_ready = sem("chunks_ready")
        at_turned = sem("at_turned")
        at_high = sem("at_high")
        at_low = sem("at_low")
        at_spread = sem("at_spread")
        at_copied = [sem("at_copied_act"), sem("at_copied_dve")]
        w_table = sem("w_table")
        x_loaded = [sem(f"x_loaded{s}") for s in range(RING)]
        xt_turned = sem("xt_turned")
        xt_copied = sem("xt_copied")
        bx_summed = sem("bx_summed")
        bx_masked = sem("bx_masked")
        bx_spread = sem("bx_spread")
        bx_copied = sem("bx_copied")
        v_made = sem("v_made")
        v_high = sem("v_high")
        v_split = sem("v_split")
        x_high = sem("x_high")
        x_low = sem("x_low")
        b_picked = sem("b_picked")
        w_picked = sem("w_picked")
        a_picked = sem("a_picked")
        w_used = sem("w_used")
        out_summed = sem("out_summed")
        y_copied = sem("y_copied")
        y_stored = [sem(f"y_stored{s}") for s in range(RING)]

        block = ctx.enter_context(nc.Block())

        def spread_bank(g):
            return ps_out[:, g // H % 2, g % H, :]

        def a_table_part(g):
            k, h = g // H, g % H
            return a_table[:, h * AH:(h + 1) * AH, :].rearrange("p n (o k) -> p k n o", k=K)[:, k, :, :]

        def past(eng, semaphore, count):
            if not isinstance(count, int) or count > 0:
                eng.wait_ge(semaphore, count)

        def turns(eng, step, ahead, first=1):
            for s in range(-ahead, RING * first):
                step(s // RING, s % RING)
            with eng.Fori(first, pairs // RING - 1) as turn:
                for s in range(RING):
                    step(turn, s)
            for s in range(RING):
                step(pairs // RING - 1, s)

        def exists(turn, s):
            return not isinstance(turn, int) or 0 <= turn * RING + s < pairs

        def batch_id(eng, which, turn, s, b):
            top = (adapters, mixes)[which] - 1
            at = (turn * RING + s) * PAIR + b
            return eng.value_load(ids[0:1, which, bass.ds(at, 1)], min_val=0, max_val=top)

        @block.sync
        def _(sp):
            sp.dma_start(ids[0:1, 0, :], adapter_id.rearrange("(a b) -> a b", a=1)).then_inc(consts_loaded, 16)
            sp.dma_start(ids[0:1, 1, :], mix_id.rearrange("(a b) -> a b", a=1)).then_inc(consts_loaded, 16)
            for dst, src in ((identity, ident), (pair_diag, pair_mask), (spread_sb, spread), (low_sb, low_rows),
                             (slot_sb, slot_part), (chunk_sb, chunk_rows)):
                sp.dma_start(dst[:], src).then_inc(consts_loaded, 16)
            sp.dma_start(b_rows[:], lora_b.rearrange("n r i -> (n r) i")).then_inc(b_loaded, 16)
            sp.dma_start(a_rows[:].rearrange("p n k r -> p n (k r)"),
                         lora_a.rearrange("n (p k) r -> p n (k r)", k=K)).then_inc(a_loaded, 16)
            for b in range(PAIR):
                sp.dma_start(w_full[b * PART:(b + 1) * PART],
                             mix_w.rearrange("m c d -> c m d")).then_inc(w_loaded, 16)

            def load(turn, s):
                if not exists(turn, s):
                    return
                n = turn * RING + s
                past(sp, xt_turned, H * (n - RING + 1))
                past(sp, x_low, n - RING + 1)
                sp.dma_start(x_sb[:, s % RING, :], x_dram[n]).then_inc(x_loaded[s % RING], 16)

            def store(turn, s):
                if not exists(turn, s):
                    return
                n = turn * RING + s
                past(sp, y_copied, H * (n + 1))
                sp.dma_start(out_dram[n], y_sb[:, s % RING, :]).then_inc(y_stored[s % RING], 16)

            def step(turn, s):
                load(turn, s + 3)
                store(turn, s - 1)

            turns(sp, step, 3)
            store(pairs // RING - 1, RING - 1)
            for s in range(RING):
                sp.wait_ge(y_stored[s], 16 * pairs // RING)

        @block.gpsimd
        def _(pool):
            def step(turn, s):
                n = turn * RING + s + 2
                if exists(turn, s + 2):
                    past(pool, x_high, n + 1)
                    past(pool, w_used, n - RING + 1)
                    q = (s + 2) % RING
                    nc.gpsimd.tensor_tensor(x_lo[:, q, :], x_sb[:, q, :], x_hi[:, q, :].bitcast(F32),
                                            ALU.subtract).then_inc(x_low, 1)

            turns(pool, step, 2)

        @block.scalar
        def _(act):
            for h in range(H):
                act.wait_ge(bt_turned, h + 1)
                nc.scalar.copy(b_table[:, h * KH:(h + 1) * KH].rearrange("p k n r -> p k (n r)"),
                               ps_xt[:, h, :].rearrange("p (k n) -> p k n", k=KH)).then_inc(bt_copied, 1)
            for h in range(H):
                act.wait_ge(at_turned, h + 1)
                nc.scalar.copy(a_turned[:, 0, h * BANK:(h + 1) * BANK], ps_out[:, 0, h, :]).then_inc(at_high, 1)
            for g in range(0, H * K, 2):
                act.wait_ge(at_spread, g + 1)
                nc.scalar.copy(a_table_part(g), spread_bank(g)).then_inc(at_copied[0], 1)

            def pick_b(turn, s):
                if not exists(turn, s):
                    return
                n = turn * RING + s
                picked = [batch_id(act, 0, turn, s, b) for b in range(PAIR)]
                past(act, bx_summed, n - 1)
                for b in range(PAIR):
                    last = nc.scalar.copy(b_pair[:, s % 2, :, b, :].rearrange("p k (n r) -> p k n r", n=1),
                                          b_table[:, :, bass.ds(picked[b], 1), :])
                last.then_inc(b_picked, 1)

            def copy_xt(turn, s, h):
                if not exists(turn, s):
                    return
                n = turn * RING + s
                past(act, xt_turned, H * n + h + 1)
                past(act, bx_summed, n - 1)
                nc.scalar.copy(x_t[:, s % 2, h * KH:(h + 1) * KH, :],
                               ps_xt[:, h, :].rearrange("p (k c) -> p k c", k=KH)).then_inc(xt_copied, 1)

            def copy_y(turn, s, h):
                if not exists(turn, s):
                    return
                n = turn * RING + s
                past(act, out_summed, H * n + h + 1)
                past(act, y_stored[s % RING], 16 * (turn + s // RING))
                nc.scalar.copy(y_sb[:, s % RING, h * BANK:(h + 1) * BANK],
                               ps_out[:, s % 2, h, :]).then_inc(y_copied, 1)

            def step(turn, s):
                n = turn * RING + s
                if exists(turn, s):
                    past(act, bx_spread, n + 1)
                    past(act, v_made, n)
                    nc.scalar.copy(bx[:], ps_s).then_inc(bx_copied, 1)
                copy_y(turn, s - 1, 0)
                copy_xt(turn, s + 1, 0)
                if exists(turn, s):
                    past(act, v_made, n + 1)
                    past(act, v_split, n)
                    nc.scalar.copy(v_hi[:], ps_v).then_inc(v_high, 1)
                copy_y(turn, s - 1, 1)
                copy_xt(turn, s + 1, 1)
                pick_b(turn, s + 2)

            turns(act, step, 2, first=2)
            for h in range(H):
                copy_y(pairs // RING - 1, RING - 1, h)

        @block.vector
        def _(dve):
            nc.vector.memset(w_pair[:], 0.0).then_inc(zeroed, 1)
            nc.vector.memset(w_pair_parts[:].bitcast(F32), 0.0).then_inc(zeroed, 1)
            dve.wait_ge(consts_loaded, 8 * 16)
            dve.wait_ge(w_loaded, PAIR * 16)
            for b in range(PAIR):
                half = slice(b * PART, (b + 1) * PART)
                eye = identity[half, half].rearrange("p (m c) -> p m c", m=1).to_broadcast([PART, mixes, C])
                nc.vector.tensor_tensor(w_full[half], w_full[half], eye, ALU.add).then_inc(w_table, 1)
            dve.wait_ge(w_table, PAIR)
            nc.vector.tensor_copy(w_parts[:, :, 0, :], w_full[:]).then_inc(w_table, 1)
            dve.wait_ge(w_table, PAIR + 1)
            nc.vector.tensor_tensor(w_parts[:, :, 1, :], w_full[:], w_parts[:, :, 0, :].bitcast(F32),
                                    ALU.subtract).then_inc(w_table, 1)
            for k in range(K):
                nc.vector.tensor_scalar(pick_chunk[:, k, :, :], slot_sb[:], chunk_sb[:, k:k + 1], None,
                                        ALU.mult).then_inc(chunks_ready, 1)
            for h in range(H):
                dve.wait_ge(at_high, h + 1)
                nc.vector.tensor_tensor(a_turned[:, 1, h * BANK:(h + 1) * BANK], ps_out[:, 0, h, :],
                                        a_turned[:, 0, h * BANK:(h + 1) * BANK].bitcast(F32),
                                        ALU.subtract).then_inc(at_low, 1)
            for g in range(1, H * K, 2):
                dve.wait_ge(at_spread, g + 1)
                nc.vector.tensor_copy(a_table_part(g), spread_bank(g)).then_inc(at_copied[1], 1)
            dve.wait_ge(w_table, PAIR + 2)
            dve.wait_ge(zeroed, 2)
            for half in at_copied:
                dve.wait_ge(half, H * K // 2)

            def high_x(turn, s):
                if not exists(turn, s):
                    return
                n = turn * RING + s
                past(dve, x_loaded[s % RING], 16 * (turn + s // RING + 1))
                past(dve, w_used, n - RING + 1)
                nc.vector.tensor_copy(x_hi[:, s % RING, :], x_sb[:, s % RING, :]).then_inc(x_high, 1)

            def pick_w(turn, s):
                if not exists(turn, s):
                    return
                n = turn * RING + s
                picked = [batch_id(dve, 1, turn, s, b) for b in range(PAIR)]
                past(dve, w_used, n - 1)
                past(dve, v_made, n - 1)
                for b in range(PAIR):
                    half = slice(b * PART, (b + 1) * PART)
                    nc.vector.tensor_copy(
                        w_pair_parts[half, s % 2, :, half].rearrange("p (m q) d -> p m q d", m=1),
                        w_parts[half, bass.ds(picked[b], 1), :, :])
                    last = nc.vector.tensor_copy(
                        w_pair[half, s % 2, half].rearrange("p (m d) -> p m d", m=1),
                        w_full[half, bass.ds(picked[b], 1), :])
                last.then_inc(w_picked, 1)

            def pick_a(turn, s):
                if not exists(turn, s):
                    return
                n = turn * RING + s
                picked = [batch_id(dve, 0, turn, s, b) for b in range(PAIR)]
                past(dve, out_summed, H * (n - 1))
                for b in range(PAIR):
                    half = slice(b * PART, (b + 1) * PART)
                    last = nc.vector.tensor_copy(
                        a_pair[half, s % 2, :].rearrange("p (n t) -> p n t", n=1),
                        a_table[half, bass.ds(picked[b], 1), :])
                last.then_inc(a_picked, 1)

            def split_v(turn, s):
                if not exists(turn, s):
                    return
                n = turn * RING + s
                past(dve, v_high, n + 1)
                past(dve, out_summed, H * (n - 1))
                nc.vector.scalar_tensor_tensor(out=v_pair[:, s % 2, :], in0=v_hi[:].bitcast(F32),
                                               scalar=low_sb[:, 0:1], in1=ps_v,
                                               op0=ALU.mult, op1=ALU.add).then_inc(v_split, 1)

            def mask_bx(turn, s):
                if not exists(turn, s):
                    return
                n = turn * RING + s
                past(dve, bx_summed, n + 1)
                past(dve, bx_spread, n)
                nc.vector.tensor_tensor(bx_t[:], ps_bx[:, 0:P], pair_diag[:], ALU.mult).then_inc(bx_masked, 1)

            def step(turn, s):
                high_x(turn, s + 2)
                pick_w(turn, s + 1)
                split_v(turn, s)
                pick_a(turn, s + 1)
                mask_bx(turn, s + 1)

            turns(dve, step, 2)

        @block.tensor
        def _(pe):
            pe.wait_ge(consts_loaded, 8 * 16)
            pe.wait_ge(b_loaded, 16)
            for h in range(H):
                for k in range(KH):
                    last = nc.tensor.transpose(ps_xt[:, h, k * P:(k + 1) * P],
                                               b_rows[:, (h * KH + k) * P:(h * KH + k + 1) * P], identity[:])
                last.then_inc(bt_turned, 1)
            pe.wait_ge(a_loaded, 16)
            for h in range(H):
                for n in range(AH):
                    last = nc.tensor.transpose(ps_out[:, 0, h, n * P:(n + 1) * P],
                                               a_rows[:, h * AH + n, :, :].rearrange("p k r -> p (k r)"),
                                               identity[:])
                last.then_inc(at_turned, 1)
            pe.wait_ge(chunks_ready, K)
            pe.wait_ge(at_low, H)
            for g in range(H * K):
                k, h = g // H, g % H
                past(pe, at_copied[g % 2], g // 2 - 1)
                for part in range(2):
                    last = nc.tensor.matmul(spread_bank(g), pick_chunk[:, k, part, :],
                                            a_turned[:, part, h * BANK:(h + 1) * BANK],
                                            start=(part == 0), stop=(part == 1))
                last.then_inc(at_spread, 1)
            for half in at_copied:
                pe.wait_ge(half, H * K // 2)
            pe.wait_ge(bt_copied, H)

            def turn_x(turn, s, h):
                if not exists(turn, s):
                    return
                n = turn * RING + s
                if h == 0:
                    past(pe, x_loaded[s % RING], 16 * (turn + s // RING + 1))
                past(pe, xt_copied, H * (n - 1) + h + 1)
                for k in range(KH):
                    at = (h * KH + k) * P
                    last = nc.tensor.transpose(ps_xt[:, h, k * P:(k + 1) * P],
                                               x_sb[:, s % RING, at:at + P], identity[:])
                last.then_inc(xt_turned, 1)

            def sum_bx(turn, s, h):
                if not exists(turn, s):
                    return
                n = turn * RING + s
                if h == 0:
                    past(pe, b_picked, n + 1)
                    past(pe, bx_masked, n)
                past(pe, xt_copied, H * n + h + 1)
                for k in range(h * KH, (h + 1) * KH):
                    g = k % 4
                    last = nc.tensor.matmul(ps_bx[g * TILE_COLS:(g + 1) * TILE_COLS, 0:P],
                                            b_pair[:, s % 2, k, :, :].rearrange("p b r -> p (b r)"),
                                            x_t[:, s % 2, k, :], start=(h == 0), stop=(h == H - 1),
                                            tile_position=(0, g * TILE_COLS))
                if h == H - 1:
                    last.then_inc(bx_summed, 1)

            def spread_bx(turn, s):
                if not exists(turn, s):
                    return
                n = turn * RING + s
                past(pe, bx_masked, n + 1)
                past(pe, bx_copied, n)
                past(pe, v_split, n)
                nc.tensor.matmul(ps_s, bx_t[:], spread_sb[:], start=True, stop=True).then_inc(bx_spread, 1)

            def make_v(turn, s):
                if not exists(turn, s):
                    return
                n = turn * RING + s
                past(pe, bx_copied, n + 1)
                past(pe, w_picked, n + 1)
                nc.tensor.matmul(ps_v, bx[:], w_pair[:, s % 2, :], start=True, stop=True).then_inc(v_made, 1)

            def mix(turn, s, h):
                if not exists(turn, s):
                    return
                n = turn * RING + s
                if h == 0:
                    past(pe, w_picked, n + 1)
                    past(pe, x_low, n + 1)
                past(pe, y_copied, H * (n - 2) + h + 1)
                cols = slice(h * BANK, (h + 1) * BANK)
                q = s % RING
                hi, lo = w_pair_parts[:, s % 2, 0, :], w_pair_parts[:, s % 2, 1, :]
                nc.tensor.matmul(ps_out[:, s % 2, h, :], hi, x_hi[:, q, cols], start=True, stop=False)
                nc.tensor.matmul(ps_out[:, s % 2, h, :], hi, x_lo[:, q, cols], start=False, stop=False)
                last = nc.tensor.matmul(ps_out[:, s % 2, h, :], lo, x_hi[:, q, cols], start=False, stop=False)
                if h == H - 1:
                    last.then_inc(w_used, 1)

            def add_adapter(turn, s, h):
                if not exists(turn, s):
                    return
                n = turn * RING + s
                if h == 0:
                    past(pe, v_split, n + 1)
                    past(pe, a_picked, n + 1)
                nc.tensor.matmul(ps_out[:, s % 2, h, :], v_pair[:, s % 2, :],
                                 a_pair[:, s % 2, h * BANK:(h + 1) * BANK],
                                 start=False, stop=True).then_inc(out_summed, 1)

            def step(turn, s):
                turn_x(turn, s + 1, 0)
                make_v(turn, s)
                mix(turn, s, 0)
                turn_x(turn, s + 1, 1)
                sum_bx(turn, s + 1, 0)
                mix(turn, s, 1)
                sum_bx(turn, s + 1, 1)
                add_adapter(turn, s, 0)
                add_adapter(turn, s, 1)
                spread_bx(turn, s + 1)

            turns(pe, step, 1)


_INS = ["x", "itok_B_3_7", "itok_B_0_15", "L0_cond_A", "L0_cond_B", "L1_cond_weights"]


def kernel(**inputs):
    import numpy as _np
    import concourse.bacc as _bacc
    from concourse import mybir as _mybir
    from concourse.bass_utils import run_bass_kernel_spmd as _run

    named = {name: _np.ascontiguousarray(inputs[name]) for name in _INS}
    rank = named["L0_cond_A"].shape[2]
    row = _np.arange(P)
    batch_of_tile_row = row % TILE_COLS // rank
    batch_of_row = row // (P // PAIR)
    slot = row // rank % SLOTS
    named["ident"] = _np.eye(P, dtype=_np.float32)
    named["pair_mask"] = (batch_of_tile_row[:, None] == batch_of_row[None, :]).astype(_np.float32)
    named["spread"] = ((batch_of_tile_row[:, None] == batch_of_row[None, :])
                       & (row[:, None] % rank == row[None, :] % rank)).astype(_np.float32)
    named["low_rows"] = -(slot // 2)[:, None].astype(_np.float32)
    same_rank = row[:, None] % rank == row[None, :] % rank
    named["slot_part"] = _np.stack([same_rank & (slot[None, :] % 2 == part) for part in range(2)], 1).astype(_np.float32)
    named["chunk_rows"] = _np.repeat(_np.eye(P // rank, dtype=_np.float32), rank, axis=0)

    nc = _bacc.Bacc("TRN2", target_bir_lowering=False, num_devices=1)
    arrays, args = {}, []
    for name, a in named.items():
        arrays[f"in_{name}_dram"] = a
        args.append(nc.dram_tensor(f"in_{name}_dram", a.shape, _mybir.dt.from_np(a.dtype), kind="ExternalInput").ap())
    shape = named["x"].shape
    args.append(nc.dram_tensor("out_0_dram", shape, _mybir.dt.float32, kind="ExternalOutput").ap())
    cond_resid_kernel(nc, *args)
    r = _run(nc, [arrays], core_ids=[0])
    return r.results[0]["out_0_dram"]
```

```python
from contextlib import ExitStack

import concourse.bass as bass
from concourse import mybir

ALU = mybir.AluOpType
F32 = mybir.dt.float32
F32R = mybir.dt.float32r
I32 = mybir.dt.int32

P = 128
PAIR = 2
RING = 4
BANK = 512
SLOTS = 4
TILE_COLS = 32


def cond_resid_kernel(nc, x, adapter_id, mix_id, lora_a, lora_b, mix_w, ident, pair_mask, spread, low_rows, slot_part,
                      chunk_rows, out):
    batches, C, T = x.shape
    adapters, _, R = lora_a.shape
    mixes = mix_w.shape[0]
    pairs = batches // PAIR
    K = T // P
    H = T // BANK
    KH = K // H
    AH = adapters // H
    PART = P // PAIR
    assert C == PART and adapters * R == P and PAIR * SLOTS * R == P and PAIR * R == TILE_COLS
    assert pairs % RING == 0 and H == 2

    x_dram = x.rearrange("(n b) c t -> n (b c) t", b=PAIR)
    out_dram = out.rearrange("(n b) c t -> n (b c) t", b=PAIR)

    with ExitStack() as ctx:
        def sb(name, shape, dt=F32):
            return ctx.enter_context(nc.sbuf_tensor(name, shape, dt))

        def psum(name, shape):
            return ctx.enter_context(nc.psum_tensor(name, shape, F32))

        def sem(name):
            return ctx.enter_context(nc.semaphore(name))

        ids_ahead = (1, 2, 2)
        ids_top = (adapters, adapters, mixes)
        ids_raw = sb("ids_raw", [1, 2, batches], I32)
        ids = sb("ids", [1, 3, batches + 4], I32)
        identity = sb("identity", [P, P])
        pair_diag = sb("pair_diag", [P, P])
        spread_sb = sb("spread_sb", [P, P])
        low_sb = sb("low_sb", [P, 1])
        slot_sb = sb("slot_sb", [P, 2, P])
        chunk_sb = sb("chunk_sb", [P, K])
        pick_chunk = sb("pick_chunk", [P, K, 2, P], F32R)
        a_turned = sb("a_turned", [P, 2, T], F32R)
        a_rows = sb("a_rows", [P, adapters, K, R])
        b_rows = sb("b_rows", [P, T])
        b_table = sb("b_table", [P, K, adapters, R])
        a_table = sb("a_table", [P, adapters, T], F32R)
        w_full = sb("w_full", [P, mixes, C])

        x_sb = sb("x_sb", [P, RING, T])
        x_hi = sb("x_hi", [P, RING, T], F32R)
        x_lo = sb("x_lo", [P, RING, T], F32R)
        x_t = sb("x_t", [P, 2, K, P])
        b_pair = sb("b_pair", [P, 2, K, PAIR, R])
        w_pair = sb("w_pair", [P, 2, P])
        w_pair_parts = sb("w_pair_parts", [P, 2, 2, P], F32R)
        a_pair = sb("a_pair", [P, 2, T], F32R)
        bx_t = sb("bx_t", [P, P])
        bx = sb("bx", [P, P])
        v_hi = sb("v_hi", [P, P], F32R)
        v_pair = sb("v_pair", [P, 2, P], F32R)
        y_sb = sb("y_sb", [P, RING, T])

        ps_xt = psum("ps_xt", [P, 2, BANK])
        ps_out = psum("ps_out", [P, 2, H, BANK])
        ps_bx = psum("ps_bx", [P, BANK])
        ps_sv = psum("ps_sv", [P, 2, P])
        ps_s, ps_v = ps_sv[:, 0, :], ps_sv[:, 1, :]

        consts_loaded = sem("consts_loaded")
        ids_loaded = sem("ids_loaded")
        ids_ready = sem("ids_ready")
        a_loaded = sem("a_loaded")
        b_loaded = sem("b_loaded")
        w_loaded = sem("w_loaded")
        zeroed = sem("zeroed")
        bt_turned = sem("bt_turned")
        bt_copied = sem("bt_copied")
        chunks_ready = sem("chunks_ready")
        at_turned = sem("at_turned")
        at_high = sem("at_high")
        at_low = sem("at_low")
        at_spread = sem("at_spread")
        at_copied = [sem("at_copied_act"), sem("at_copied_dve")]
        w_table = sem("w_table")
        x_loaded = [sem(f"x_loaded{s}") for s in range(RING)]
        xt_turned = sem("xt_turned")
        xt_copied = sem("xt_copied")
        bx_summed = sem("bx_summed")
        bx_masked = sem("bx_masked")
        bx_spread = sem("bx_spread")
        bx_copied = sem("bx_copied")
        v_made = sem("v_made")
        v_high = sem("v_high")
        v_split = sem("v_split")
        x_high = sem("x_high")
        x_low = sem("x_low")
        b_picked = sem("b_picked")
        w_picked = sem("w_picked")
        w_high = sem("w_high")
        w_split = sem("w_split")
        a_picked = sem("a_picked")
        w_used = sem("w_used")
        out_summed = sem("out_summed")
        y_copied = sem("y_copied")
        y_stored = [sem(f"y_stored{s}") for s in range(RING)]

        block = ctx.enter_context(nc.Block())

        def spread_bank(g):
            return ps_out[:, g // H % 2, g % H, :]

        def a_table_part(g):
            k, h = g // H, g % H
            return a_table[:, h * AH:(h + 1) * AH, :].rearrange("p n (o k) -> p k n o", k=K)[:, k, :, :]

        def past(eng, semaphore, count):
            if not isinstance(count, int) or count > 0:
                eng.wait_ge(semaphore, count)

        def turns(eng, step, ahead, first=1, users=()):
            def steps(turn, s):
                ids_of = {user: turn_ids(eng, user, turn, s) for user in users}
                for t in range(s, RING):
                    step(turn, t, *(ids_of[user].get(t) for user in users))

            steps(-1, RING - ahead)
            for turn in range(first):
                steps(turn, 0)
            with eng.Fori(first, pairs // RING - 1) as turn:
                steps(turn, 0)
            steps(pairs // RING - 1, 0)

        def exists(turn, s):
            return not isinstance(turn, int) or 0 <= turn * RING + s < pairs

        def id_column(user):
            return ids_ahead[user] % 2 * PAIR

        def turn_ids(eng, user, turn, s):
            first = turn * RING + s + ids_ahead[user]
            steps = range(s, RING)
            if isinstance(turn, int):
                steps = [t for t in steps if exists(turn, t + ids_ahead[user])]
                first = turn * RING + min(steps, default=0) + ids_ahead[user]
            if not steps:
                return {}
            at = first * PAIR + id_column(user)
            _, values = nc.values_load_multi_w_load_instructions(
                ids[0:1, user, bass.ds(at, PAIR * len(steps))], engines=[eng.engine], min_val=0,
                max_val=ids_top[user] - 1, skip_runtime_bounds_check_because="the ids were clamped to the table")
            return {t: values[PAIR * i:PAIR * (i + 1)] for i, t in enumerate(steps)}

        @block.sync
        def _(sp):
            for kind, source in enumerate((adapter_id, mix_id)):
                sp.dma_start(ids_raw[0:1, kind, :], source.rearrange("(a b) -> a b", a=1)).then_inc(ids_loaded, 16)
            for dst, src in ((identity, ident), (pair_diag, pair_mask), (spread_sb, spread), (low_sb, low_rows),
                             (slot_sb, slot_part), (chunk_sb, chunk_rows)):
                sp.dma_start(dst[:], src).then_inc(consts_loaded, 16)
            sp.dma_start(b_rows[:], lora_b.rearrange("n r i -> (n r) i")).then_inc(b_loaded, 16)
            sp.dma_start(a_rows[:].rearrange("p n k r -> p n (k r)"),
                         lora_a.rearrange("n (p k) r -> p n (k r)", k=K)).then_inc(a_loaded, 16)
            for b in range(PAIR):
                sp.dma_start(w_full[b * PART:(b + 1) * PART],
                             mix_w.rearrange("m c d -> c m d")).then_inc(w_loaded, 16)

            def load(turn, s):
                if not exists(turn, s):
                    return
                n = turn * RING + s
                past(sp, xt_turned, H * (n - RING + 1))
                past(sp, x_low, n - RING + 1)
                sp.dma_start(x_sb[:, s % RING, :], x_dram[n]).then_inc(x_loaded[s % RING], 16)

            def store(turn, s):
                if not exists(turn, s):
                    return
                n = turn * RING + s
                past(sp, y_copied, H * (n + 1))
                sp.dma_start(out_dram[n], y_sb[:, s % RING, :]).then_inc(y_stored[s % RING], 16)

            def step(turn, s):
                load(turn, s + 3)
                store(turn, s - 1)

            turns(sp, step, 3)
            store(pairs // RING - 1, RING - 1)
            for s in range(RING):
                sp.wait_ge(y_stored[s], 16 * pairs // RING)

        @block.gpsimd
        def _(pool):
            def step(turn, s):
                n = turn * RING + s + 2
                if exists(turn, s + 2):
                    past(pool, x_high, n + 1)
                    past(pool, w_used, n - RING + 1)
                    q = (s + 2) % RING
                    nc.gpsimd.tensor_tensor(x_lo[:, q, :], x_sb[:, q, :], x_hi[:, q, :].bitcast(F32),
                                            ALU.subtract).then_inc(x_low, 1)

            turns(pool, step, 2)

        @block.scalar
        def _(act):
            for h in range(H):
                act.wait_ge(bt_turned, h + 1)
                nc.scalar.copy(b_table[:, h * KH:(h + 1) * KH].rearrange("p k n r -> p k (n r)"),
                               ps_xt[:, h, :].rearrange("p (k n) -> p k n", k=KH)).then_inc(bt_copied, 1)
            for h in range(H):
                act.wait_ge(at_turned, h + 1)
                nc.scalar.copy(a_turned[:, 0, h * BANK:(h + 1) * BANK], ps_out[:, 0, h, :]).then_inc(at_high, 1)
            for g in range(0, H * K, 2):
                act.wait_ge(at_spread, g + 1)
                nc.scalar.copy(a_table_part(g), spread_bank(g)).then_inc(at_copied[0], 1)

            act.wait_ge(ids_ready, 3)
            act.wait_ge(w_table, PAIR)
            act.wait_ge(zeroed, 1)

            def pick_w(turn, s, picked):
                if not exists(turn, s):
                    return
                n = turn * RING + s
                past(act, v_made, n - 1)
                past(act, w_split, n - 1)
                for b in range(PAIR):
                    half = slice(b * PART, (b + 1) * PART)
                    last = nc.scalar.copy(w_pair[half, s % 2, half].rearrange("p (m d) -> p m d", m=1),
                                          w_full[half, bass.ds(picked[b], 1), :])
                last.then_inc(w_picked, 1)

            def pick_b(turn, s, picked):
                if not exists(turn, s):
                    return
                n = turn * RING + s
                past(act, bx_summed, n - 1)
                for b in range(PAIR):
                    last = nc.scalar.copy(b_pair[:, s % 2, :, b, :].rearrange("p k (n r) -> p k n r", n=1),
                                          b_table[:, :, bass.ds(picked[b], 1), :])
                last.then_inc(b_picked, 1)

            def copy_xt(turn, s, h):
                if not exists(turn, s):
                    return
                n = turn * RING + s
                past(act, xt_turned, H * n + h + 1)
                past(act, bx_summed, n - 1)
                nc.scalar.copy(x_t[:, s % 2, h * KH:(h + 1) * KH, :],
                               ps_xt[:, h, :].rearrange("p (k c) -> p k c", k=KH)).then_inc(xt_copied, 1)

            def copy_y(turn, s, h):
                if not exists(turn, s):
                    return
                n = turn * RING + s
                past(act, out_summed, H * n + h + 1)
                past(act, y_stored[s % RING], 16 * (turn + s // RING))
                nc.scalar.copy(y_sb[:, s % RING, h * BANK:(h + 1) * BANK],
                               ps_out[:, s % 2, h, :]).then_inc(y_copied, 1)

            def step(turn, s, next_adapters, next_mixes):
                n = turn * RING + s
                copy_y(turn, s - 1, 0)
                if exists(turn, s):
                    past(act, bx_spread, n + 1)
                    past(act, v_made, n)
                    nc.scalar.copy(bx[:], ps_s).then_inc(bx_copied, 1)
                copy_xt(turn, s + 1, 0)
                copy_y(turn, s - 1, 1)
                if exists(turn, s):
                    past(act, v_made, n + 1)
                    past(act, v_split, n)
                    nc.scalar.copy(v_hi[:], ps_v).then_inc(v_high, 1)
                copy_xt(turn, s + 1, 1)
                pick_b(turn, s + 2, next_adapters)
                pick_w(turn, s + 2, next_mixes)

            turns(act, step, 2, first=2, users=(1, 2))
            for h in range(H):
                copy_y(pairs // RING - 1, RING - 1, h)

        @block.vector
        def _(dve):
            nc.vector.memset(w_pair[:], 0.0).then_inc(zeroed, 1)
            dve.wait_ge(ids_loaded, 2 * 16)
            for user in range(3):
                nc.vector.tensor_scalar(ids[0:1, user, id_column(user):id_column(user) + batches],
                                        ids_raw[0:1, user // 2, :], 0, ids_top[user] - 1,
                                        ALU.max, ALU.min).then_inc(ids_ready, 1)
            dve.wait_ge(consts_loaded, 6 * 16)
            dve.wait_ge(w_loaded, PAIR * 16)
            for b in range(PAIR):
                half = slice(b * PART, (b + 1) * PART)
                eye = identity[half, half].rearrange("p (m c) -> p m c", m=1).to_broadcast([PART, mixes, C])
                nc.vector.tensor_tensor(w_full[half], w_full[half], eye, ALU.add).then_inc(w_table, 1)
            for k in range(K):
                nc.vector.tensor_scalar(pick_chunk[:, k, :, :], slot_sb[:], chunk_sb[:, k:k + 1], None,
                                        ALU.mult).then_inc(chunks_ready, 1)
            for h in range(H):
                dve.wait_ge(at_high, h + 1)
                nc.vector.tensor_tensor(a_turned[:, 1, h * BANK:(h + 1) * BANK], ps_out[:, 0, h, :],
                                        a_turned[:, 0, h * BANK:(h + 1) * BANK].bitcast(F32),
                                        ALU.subtract).then_inc(at_low, 1)
            for g in range(1, H * K, 2):
                dve.wait_ge(at_spread, g + 1)
                nc.vector.tensor_copy(a_table_part(g), spread_bank(g)).then_inc(at_copied[1], 1)
            dve.wait_ge(ids_ready, 3)
            for half in at_copied:
                dve.wait_ge(half, H * K // 2)

            def high_x(turn, s):
                if not exists(turn, s):
                    return
                n = turn * RING + s
                past(dve, x_loaded[s % RING], 16 * (turn + s // RING + 1))
                past(dve, w_used, n - RING + 1)
                nc.vector.tensor_copy(x_hi[:, s % RING, :], x_sb[:, s % RING, :]).then_inc(x_high, 1)

            def split_w(turn, s):
                if not exists(turn, s):
                    return
                n = turn * RING + s
                past(dve, w_picked, n + 1)
                past(dve, w_used, n - 1)
                hi, lo = w_pair_parts[:, s % 2, 0, :], w_pair_parts[:, s % 2, 1, :]
                nc.vector.tensor_copy(hi, w_pair[:, s % 2, :]).then_inc(w_high, 1)
                past(dve, w_high, n + 1)
                nc.vector.tensor_tensor(lo, w_pair[:, s % 2, :], hi.bitcast(F32), ALU.subtract).then_inc(w_split, 1)

            def pick_a(turn, s, picked):
                if not exists(turn, s):
                    return
                n = turn * RING + s
                past(dve, out_summed, H * (n - 1))
                for b in range(PAIR):
                    half = slice(b * PART, (b + 1) * PART)
                    last = nc.vector.tensor_copy(
                        a_pair[half, s % 2, :].rearrange("p (n t) -> p n t", n=1),
                        a_table[half, bass.ds(picked[b], 1), :])
                last.then_inc(a_picked, 1)

            def split_v(turn, s):
                if not exists(turn, s):
                    return
                n = turn * RING + s
                past(dve, v_high, n + 1)
                past(dve, out_summed, H * (n - 1))
                nc.vector.scalar_tensor_tensor(out=v_pair[:, s % 2, :], in0=v_hi[:].bitcast(F32),
                                               scalar=low_sb[:, 0:1], in1=ps_v,
                                               op0=ALU.mult, op1=ALU.add).then_inc(v_split, 1)

            def mask_bx(turn, s):
                if not exists(turn, s):
                    return
                n = turn * RING + s
                past(dve, bx_summed, n + 1)
                past(dve, bx_spread, n)
                nc.vector.tensor_tensor(bx_t[:], ps_bx[:, 0:P], pair_diag[:], ALU.mult).then_inc(bx_masked, 1)

            def step(turn, s, next_adapters):
                high_x(turn, s + 2)
                pick_a(turn, s + 1, next_adapters)
                split_w(turn, s + 1)
                split_v(turn, s)
                mask_bx(turn, s + 1)

            turns(dve, step, 2, users=(0,))

        @block.tensor
        def _(pe):
            pe.wait_ge(consts_loaded, 6 * 16)
            pe.wait_ge(b_loaded, 16)
            for h in range(H):
                for k in range(KH):
                    last = nc.tensor.transpose(ps_xt[:, h, k * P:(k + 1) * P],
                                               b_rows[:, (h * KH + k) * P:(h * KH + k + 1) * P], identity[:])
                last.then_inc(bt_turned, 1)
            pe.wait_ge(a_loaded, 16)
            for h in range(H):
                for n in range(AH):
                    last = nc.tensor.transpose(ps_out[:, 0, h, n * P:(n + 1) * P],
                                               a_rows[:, h * AH + n, :, :].rearrange("p k r -> p (k r)"),
                                               identity[:])
                last.then_inc(at_turned, 1)
            pe.wait_ge(chunks_ready, K)
            pe.wait_ge(at_low, H)
            for g in range(H * K):
                k, h = g // H, g % H
                past(pe, at_copied[g % 2], g // 2 - 1)
                for part in range(2):
                    last = nc.tensor.matmul(spread_bank(g), pick_chunk[:, k, part, :],
                                            a_turned[:, part, h * BANK:(h + 1) * BANK],
                                            start=(part == 0), stop=(part == 1))
                last.then_inc(at_spread, 1)
            for half in at_copied:
                pe.wait_ge(half, H * K // 2)
            pe.wait_ge(bt_copied, H)

            def turn_x(turn, s, h):
                if not exists(turn, s):
                    return
                n = turn * RING + s
                if h == 0:
                    past(pe, x_loaded[s % RING], 16 * (turn + s // RING + 1))
                past(pe, xt_copied, H * (n - 1) + h + 1)
                for k in range(KH):
                    at = (h * KH + k) * P
                    last = nc.tensor.transpose(ps_xt[:, h, k * P:(k + 1) * P],
                                               x_sb[:, s % RING, at:at + P], identity[:])
                last.then_inc(xt_turned, 1)

            def sum_bx(turn, s, h):
                if not exists(turn, s):
                    return
                n = turn * RING + s
                if h == 0:
                    past(pe, b_picked, n + 1)
                    past(pe, bx_masked, n)
                past(pe, xt_copied, H * n + h + 1)
                for k in range(h * KH, (h + 1) * KH):
                    g = k % 4
                    last = nc.tensor.matmul(ps_bx[g * TILE_COLS:(g + 1) * TILE_COLS, 0:P],
                                            b_pair[:, s % 2, k, :, :].rearrange("p b r -> p (b r)"),
                                            x_t[:, s % 2, k, :], start=(h == 0), stop=(h == H - 1),
                                            tile_position=(0, g * TILE_COLS))
                if h == H - 1:
                    last.then_inc(bx_summed, 1)

            def spread_bx(turn, s):
                if not exists(turn, s):
                    return
                n = turn * RING + s
                past(pe, bx_masked, n + 1)
                past(pe, bx_copied, n)
                past(pe, v_split, n)
                nc.tensor.matmul(ps_s, bx_t[:], spread_sb[:], start=True, stop=True).then_inc(bx_spread, 1)

            def make_v(turn, s):
                if not exists(turn, s):
                    return
                n = turn * RING + s
                past(pe, bx_copied, n + 1)
                past(pe, w_picked, n + 1)
                nc.tensor.matmul(ps_v, bx[:], w_pair[:, s % 2, :], start=True, stop=True).then_inc(v_made, 1)

            def mix(turn, s, h):
                if not exists(turn, s):
                    return
                n = turn * RING + s
                if h == 0:
                    past(pe, w_split, n + 1)
                    past(pe, x_low, n + 1)
                past(pe, y_copied, H * (n - 2) + h + 1)
                cols = slice(h * BANK, (h + 1) * BANK)
                q = s % RING
                hi, lo = w_pair_parts[:, s % 2, 0, :], w_pair_parts[:, s % 2, 1, :]
                nc.tensor.matmul(ps_out[:, s % 2, h, :], hi, x_hi[:, q, cols], start=True, stop=False)
                nc.tensor.matmul(ps_out[:, s % 2, h, :], hi, x_lo[:, q, cols], start=False, stop=False)
                last = nc.tensor.matmul(ps_out[:, s % 2, h, :], lo, x_hi[:, q, cols], start=False, stop=False)
                if h == H - 1:
                    last.then_inc(w_used, 1)

            def add_adapter(turn, s, h):
                if not exists(turn, s):
                    return
                n = turn * RING + s
                if h == 0:
                    past(pe, v_split, n + 1)
                    past(pe, a_picked, n + 1)
                nc.tensor.matmul(ps_out[:, s % 2, h, :], v_pair[:, s % 2, :],
                                 a_pair[:, s % 2, h * BANK:(h + 1) * BANK],
                                 start=False, stop=True).then_inc(out_summed, 1)

            def step(turn, s):
                turn_x(turn, s + 1, 0)
                spread_bx(turn, s)
                mix(turn, s, 0)
                make_v(turn, s)
                turn_x(turn, s + 1, 1)
                sum_bx(turn, s + 1, 0)
                mix(turn, s, 1)
                sum_bx(turn, s + 1, 1)
                add_adapter(turn, s, 0)
                add_adapter(turn, s, 1)

            turns(pe, step, 1)


_INS = ["x", "itok_B_3_7", "itok_B_0_15", "L0_cond_A", "L0_cond_B", "L1_cond_weights"]


def kernel(**inputs):
    import numpy as _np
    import concourse.bacc as _bacc
    from concourse import mybir as _mybir
    from concourse.bass_utils import run_bass_kernel_spmd as _run

    named = {name: _np.ascontiguousarray(inputs[name]) for name in _INS}
    rank = named["L0_cond_A"].shape[2]
    row = _np.arange(P)
    batch_of_tile_row = row % TILE_COLS // rank
    batch_of_row = row // (P // PAIR)
    slot = row // rank % SLOTS
    named["ident"] = _np.eye(P, dtype=_np.float32)
    named["pair_mask"] = (batch_of_tile_row[:, None] == batch_of_row[None, :]).astype(_np.float32)
    named["spread"] = ((batch_of_tile_row[:, None] == batch_of_row[None, :])
                       & (row[:, None] % rank == row[None, :] % rank)).astype(_np.float32)
    named["low_rows"] = -(slot // 2)[:, None].astype(_np.float32)
    same_rank = row[:, None] % rank == row[None, :] % rank
    named["slot_part"] = _np.stack([same_rank & (slot[None, :] % 2 == part) for part in range(2)], 1).astype(_np.float32)
    named["chunk_rows"] = _np.repeat(_np.eye(P // rank, dtype=_np.float32), rank, axis=0)

    nc = _bacc.Bacc("TRN2", target_bir_lowering=False, num_devices=1)
    arrays, args = {}, []
    for name, a in named.items():
        arrays[f"in_{name}_dram"] = a
        args.append(nc.dram_tensor(f"in_{name}_dram", a.shape, _mybir.dt.from_np(a.dtype), kind="ExternalInput").ap())
    shape = named["x"].shape
    args.append(nc.dram_tensor("out_0_dram", shape, _mybir.dt.float32, kind="ExternalOutput").ap())
    cond_resid_kernel(nc, *args)
    r = _run(nc, [arrays], core_ids=[0])
    return r.results[0]["out_0_dram"]
```

```python
from contextlib import ExitStack

import concourse.bass as bass
from concourse import mybir

ALU = mybir.AluOpType
F32 = mybir.dt.float32
F32R = mybir.dt.float32r
I32 = mybir.dt.int32

P = 128
PAIR = 2
RING = 4
BANK = 512
SLOTS = 4
TILE_COLS = 32


def cond_resid_kernel(nc, x, adapter_id, mix_id, lora_a, lora_b, mix_w, ident, low_rows, slot_part,
                      chunk_rows, out):
    batches, C, T = x.shape
    adapters, _, R = lora_a.shape
    mixes = mix_w.shape[0]
    pairs = batches // PAIR
    K = T // P
    H = T // BANK
    KH = K // H
    AH = adapters // H
    PART = P // PAIR
    assert C == PART and adapters * R == P and PAIR * SLOTS * R == P and PAIR * R == TILE_COLS
    assert pairs % RING == 0 and H == 2

    x_dram = x.rearrange("(n b) c t -> n (b c) t", b=PAIR)
    out_dram = out.rearrange("(n b) c t -> n (b c) t", b=PAIR)

    with ExitStack() as ctx:
        def sb(name, shape, dt=F32):
            return ctx.enter_context(nc.sbuf_tensor(name, shape, dt))

        def psum(name, shape):
            return ctx.enter_context(nc.psum_tensor(name, shape, F32))

        def sem(name):
            return ctx.enter_context(nc.semaphore(name))

        PICK_A, PICK_B, PICK_W = range(3)
        ids_ahead = (0, 2, 2)
        ids_kind = (0, 0, 1)
        ids_top = (adapters, mixes)
        ids_raw = sb("ids_raw", [1, 2, batches], I32)
        unread = sb("unread", [1, 1])
        idle_rows = sb("idle_rows", [P, BANK], mybir.dt.bfloat16)
        ids = sb("ids", [1, 2, batches], I32)
        identity = sb("identity", [P, P])
        low_sb = sb("low_sb", [P, 1])
        slot_sb = sb("slot_sb", [P, 2, P])
        chunk_sb = sb("chunk_sb", [P, K])
        pick_chunk = sb("pick_chunk", [P, K, 2, P], F32R)
        a_turned = sb("a_turned", [P, 2, T], F32R)
        a_rows = sb("a_rows", [P, adapters, K, R])
        b_rows = sb("b_rows", [P, T])
        b_table = sb("b_table", [P, K, adapters, R])
        a_table = sb("a_table", [P, adapters, T], F32R)
        w_full = sb("w_full", [P, mixes, C])

        x_sb = sb("x_sb", [P, RING, T])
        x_hi = sb("x_hi", [P, RING, T], F32R)
        x_lo = sb("x_lo", [P, RING, T], F32R)
        x_t = sb("x_t", [P, 2, K, P])
        b_pair = sb("b_pair", [P, 2, K, PAIR, R])
        w_pair = sb("w_pair", [P, 2, P])
        w_pair_parts = sb("w_pair_parts", [P, 2, 2, P], F32R)
        a_pair = sb("a_pair", [P, 2, T], F32R)
        bx_t = sb("bx_t", [P, P])
        bx_sum = sb("bx_sum", [P, PAIR, R])
        bx = sb("bx", [P, P])
        v_hi = sb("v_hi", [P, P], F32R)
        v_pair = sb("v_pair", [P, 2, P], F32R)
        y_sb = sb("y_sb", [P, RING, T])

        ps_xt = psum("ps_xt", [P, 2, BANK])
        ps_out = psum("ps_out", [P, 2, H, BANK])
        ps_bx = psum("ps_bx", [P, BANK])
        ps_sv = psum("ps_sv", [P, 2, P])
        ps_s, ps_v = ps_sv[:, 0, :], ps_sv[:, 1, :]

        consts_loaded = sem("consts_loaded")
        ids_loaded = sem("ids_loaded")
        identity_loaded = sem("identity_loaded")
        slots_loaded = sem("slots_loaded")
        idle_ready = sem("idle_ready")
        ids_ready = sem("ids_ready")
        a_loaded = sem("a_loaded")
        b_loaded = sem("b_loaded")
        w_loaded = sem("w_loaded")
        zeroed = sem("zeroed")
        bt_turned = sem("bt_turned")
        bt_copied = sem("bt_copied")
        chunks_ready = sem("chunks_ready")
        at_turned = sem("at_turned")
        at_high = sem("at_high")
        at_low = sem("at_low")
        at_spread = sem("at_spread")
        at_copied = [sem("at_copied_act"), sem("at_copied_dve")]
        w_table = sem("w_table")
        x_loaded = [sem(f"x_loaded{s}") for s in range(RING)]
        xt_turned = sem("xt_turned")
        xt_copied = sem("xt_copied")
        bx_summed = sem("bx_summed")
        bxt_copied = sem("bxt_copied")
        bx_turned = sem("bx_turned")
        bx_added = sem("bx_added")
        bx_spread = sem("bx_spread")
        v_made = sem("v_made")
        v_high = sem("v_high")
        v_split = sem("v_split")
        x_high = sem("x_high")
        x_low = sem("x_low")
        b_picked = sem("b_picked")
        w_picked = sem("w_picked")
        w_high = sem("w_high")
        w_split = sem("w_split")
        a_picked = sem("a_picked")
        w_used = sem("w_used")
        out_summed = sem("out_summed")
        y_copied = sem("y_copied")
        y_stored = [sem(f"y_stored{s}") for s in range(RING)]

        block = ctx.enter_context(nc.Block())

        def spread_bank(g):
            return ps_out[:, g // H % 2, g % H, :]

        def a_table_part(g):
            k, h = g // H, g % H
            return a_table[:, h * AH:(h + 1) * AH, :].rearrange("p n (o k) -> p k n o", k=K)[:, k, :, :]

        SPREAD_FIRST = 3 * H * K // 4

        def past(eng, semaphore, count):
            if not isinstance(count, int) or count > 0:
                eng.wait_ge(semaphore, count)

        def turn_steps(eng, step, turn, s):
            ids_of = {}

            def picked(user, t):
                if user not in ids_of:
                    ids_of[user] = turn_ids(eng, user, turn, s)
                return ids_of[user][t]

            for t in range(s, RING):
                step(turn, t, picked)

        def lead_in(eng, step, ahead):
            turn_steps(eng, step, -1, RING - ahead)

        def turns(eng, step, first=1):
            for turn in range(first):
                turn_steps(eng, step, turn, 0)
            with eng.Fori(first, pairs // RING - 1) as turn:
                turn_steps(eng, step, turn, 0)
            turn_steps(eng, step, pairs // RING - 1, 0)

        def exists(turn, s):
            return not isinstance(turn, int) or 0 <= turn * RING + s < pairs

        def turn_ids(eng, user, turn, s):
            first = turn * RING + s + ids_ahead[user]
            steps = range(s, RING)
            if isinstance(turn, int):
                steps = [t for t in steps if exists(turn, t + ids_ahead[user])]
                first = turn * RING + min(steps, default=0) + ids_ahead[user]
            if not steps:
                return {}
            _, values = nc.values_load_multi_w_load_instructions(
                ids[0:1, ids_kind[user], bass.ds(first * PAIR, PAIR * len(steps))], engines=[eng.engine], min_val=0,
                max_val=ids_top[ids_kind[user]] - 1, skip_runtime_bounds_check_because="the ids were clamped to the table")
            return {t: values[PAIR * i:PAIR * (i + 1)] for i, t in enumerate(steps)}

        @block.sync
        def _(sp):
            sp.dma_start(identity[:], ident).then_inc(identity_loaded, 16)
            sp.dma_start(a_rows[:].rearrange("p n k r -> p n (k r)"),
                         lora_a.rearrange("n (p k) r -> p n (k r)", k=K)).then_inc(a_loaded, 16)
            sp.dma_start(b_rows[:], lora_b.rearrange("n r i -> (n r) i")).then_inc(b_loaded, 16)
            for b in range(PAIR):
                sp.dma_start(w_full[b * PART:(b + 1) * PART],
                             mix_w.rearrange("m c d -> c m d")).then_inc(w_loaded, 16)

            def load(turn, s):
                if not exists(turn, s):
                    return
                n = turn * RING + s
                past(sp, xt_turned, H * (n - RING + 1))
                past(sp, x_low, n - RING + 1)
                sp.dma_start(x_sb[:, s % RING, :], x_dram[n]).then_inc(x_loaded[s % RING], 16)

            def store(turn, s):
                if not exists(turn, s):
                    return
                n = turn * RING + s
                past(sp, y_copied, H * (n + 1))
                sp.dma_start(out_dram[n], y_sb[:, s % RING, :]).then_inc(y_stored[s % RING], 16)

            def step(turn, s, _):
                load(turn, s + 3)
                store(turn, s - 1)

            lead_in(sp, step, 3)
            turns(sp, step)
            store(pairs // RING - 1, RING - 1)
            for s in range(RING):
                sp.wait_ge(y_stored[s], 16 * pairs // RING)

        @block.gpsimd
        def _(pool):
            nc.gpsimd.memset(idle_rows[:], 0.0).then_inc(idle_ready, 1)
            nc.gpsimd.memset(w_pair[:], 0.0).then_inc(zeroed, 1)
            def step(turn, s, _):
                n = turn * RING + s + 2
                if exists(turn, s + 2):
                    past(pool, x_high, n + 1)
                    past(pool, w_used, n - RING + 1)
                    q = (s + 2) % RING
                    nc.gpsimd.tensor_tensor(x_lo[:, q, :], x_sb[:, q, :], x_hi[:, q, :].bitcast(F32),
                                            ALU.subtract).then_inc(x_low, 1)

            lead_in(pool, step, 2)
            turns(pool, step)

        @block.scalar
        def _(act):
            for dst, src in ((slot_sb, slot_part), (chunk_sb, chunk_rows)):
                act.dma_start(dst[:], src).then_inc(slots_loaded, 16)
            for kind, source in enumerate((adapter_id, mix_id)):
                act.dma_start(ids_raw[0:1, kind, :], source.rearrange("(a b) -> a b", a=1)).then_inc(ids_loaded, 16)
            act.dma_start(low_sb[:], low_rows).then_inc(consts_loaded, 16)
            act.wait_ge(identity_loaded, 16)
            nc.scalar.copy(unread[:], identity[0:1, 0:1])
            for h in range(H):
                act.wait_ge(at_turned, h + 1)
                nc.scalar.copy(a_turned[:, 0, h * BANK:(h + 1) * BANK], ps_out[:, 0, h, :]).then_inc(at_high, 1)
            for h in range(H):
                act.wait_ge(bt_turned, h + 1)
                nc.scalar.copy(b_table[:, h * KH:(h + 1) * KH].rearrange("p k n r -> p k (n r)"),
                               ps_xt[:, h, :].rearrange("p (k n) -> p k n", k=KH)).then_inc(bt_copied, 1)
            act.wait_ge(ids_ready, 2)
            act.wait_ge(w_table, PAIR)
            act.wait_ge(bt_copied, H)
            act.wait_ge(zeroed, 2)

            def pick_w(turn, s, picked):
                if not exists(turn, s):
                    return
                n = turn * RING + s
                chosen = picked(PICK_W, s - ids_ahead[PICK_W])
                past(act, v_made, n - 1)
                past(act, w_split, n - 1)
                for b in range(PAIR):
                    half = slice(b * PART, (b + 1) * PART)
                    last = nc.scalar.copy(w_pair[half, s % 2, half].rearrange("p (m d) -> p m d", m=1),
                                          w_full[half, bass.ds(chosen[b], 1), :])
                last.then_inc(w_picked, 1)

            def pick_b(turn, s, picked):
                if not exists(turn, s):
                    return
                n = turn * RING + s
                chosen = picked(PICK_B, s - ids_ahead[PICK_B])
                past(act, bx_summed, n - 1)
                for b in range(PAIR):
                    last = nc.scalar.copy(b_pair[:, s % 2, :, b, :].rearrange("p k (n r) -> p k n r", n=1),
                                          b_table[:, :, bass.ds(chosen[b], 1), :])
                last.then_inc(b_picked, 1)

            def copy_xt(turn, s, h):
                if not exists(turn, s):
                    return
                n = turn * RING + s
                past(act, xt_turned, H * n + h + 1)
                past(act, bx_summed, n - 1)
                nc.scalar.copy(x_t[:, s % 2, h * KH:(h + 1) * KH, :],
                               ps_xt[:, h, :].rearrange("p (k c) -> p k c", k=KH)).then_inc(xt_copied, 1)

            def copy_y(turn, s, h):
                if not exists(turn, s):
                    return
                n = turn * RING + s
                past(act, out_summed, H * n + h + 1)
                past(act, y_stored[s % RING], 16 * (turn + s // RING))
                nc.scalar.copy(y_sb[:, s % RING, h * BANK:(h + 1) * BANK],
                               ps_out[:, s % 2, h, :]).then_inc(y_copied, 1)

            def spread_bx(turn, s):
                if not exists(turn, s):
                    return
                n = turn * RING + s
                past(act, bx_added, n + 1)
                past(act, v_made, n)
                nc.scalar.copy(bx[:].rearrange("p (b q r) -> p b q r", b=PAIR, q=SLOTS),
                               bx_sum[:].rearrange("p b (q r) -> p b q r", q=1)
                               .to_broadcast([P, PAIR, SLOTS, R])).then_inc(bx_spread, 1)

            def high_v(turn, s):
                if not exists(turn, s):
                    return
                n = turn * RING + s
                past(act, v_made, n + 1)
                past(act, v_split, n)
                nc.scalar.copy(v_hi[:], ps_v).then_inc(v_high, 1)

            def step(turn, s, picked):
                copy_xt(turn, s + 1, 0)
                copy_y(turn, s - 1, 0)
                spread_bx(turn, s)
                copy_y(turn, s - 1, 1)
                copy_xt(turn, s + 1, 1)
                pick_b(turn, s + 2, picked)
                high_v(turn, s)
                pick_w(turn, s + 2, picked)

            def copy_a_table(steps):
                for g in steps:
                    act.wait_ge(at_spread, g + 1)
                    nc.scalar.copy(a_table_part(g), spread_bank(g)).then_inc(at_copied[0], 1)

            copy_a_table(range(0, SPREAD_FIRST, 2))
            lead_in(act, step, 2)
            copy_a_table(range(SPREAD_FIRST, H * K, 2))
            turns(act, step, first=2)
            for h in range(H):
                copy_y(pairs // RING - 1, RING - 1, h)

        @block.vector
        def _(dve):
            dve.wait_ge(slots_loaded, 2 * 16)
            for k in range(K):
                nc.vector.tensor_scalar(pick_chunk[:, k, :, :], slot_sb[:], chunk_sb[:, k:k + 1], None,
                                        ALU.mult).then_inc(chunks_ready, 1)
            for h in range(H):
                dve.wait_ge(at_high, h + 1)
                nc.vector.tensor_tensor(a_turned[:, 1, h * BANK:(h + 1) * BANK], ps_out[:, 0, h, :],
                                        a_turned[:, 0, h * BANK:(h + 1) * BANK].bitcast(F32),
                                        ALU.subtract).then_inc(at_low, 1)
            nc.vector.memset(ps_v, 0.0).then_inc(zeroed, 1)
            dve.wait_ge(ids_loaded, 2 * 16)
            for kind in range(2):
                nc.vector.tensor_scalar(ids[0:1, kind, :], ids_raw[0:1, kind, :], 0, ids_top[kind] - 1,
                                        ALU.max, ALU.min).then_inc(ids_ready, 1)
            def high_x(turn, s):
                if not exists(turn, s):
                    return
                n = turn * RING + s
                past(dve, x_loaded[s % RING], 16 * (turn + s // RING + 1))
                past(dve, w_used, n - RING + 1)
                nc.vector.tensor_copy(x_hi[:, s % RING, :], x_sb[:, s % RING, :]).then_inc(x_high, 1)

            def split_w(turn, s):
                if not exists(turn, s):
                    return
                n = turn * RING + s
                past(dve, w_picked, n + 1)
                past(dve, w_used, n - 1)
                hi, lo = w_pair_parts[:, s % 2, 0, :], w_pair_parts[:, s % 2, 1, :]
                nc.vector.tensor_copy(hi, w_pair[:, s % 2, :]).then_inc(w_high, 1)
                past(dve, w_high, n + 1)
                nc.vector.tensor_tensor(lo, w_pair[:, s % 2, :], hi.bitcast(F32), ALU.subtract).then_inc(w_split, 1)

            def pick_a(turn, s, picked):
                if not exists(turn, s):
                    return
                n = turn * RING + s
                chosen = picked(PICK_A, s - ids_ahead[PICK_A])
                past(dve, out_summed, H * (n - 1))
                for b in range(PAIR):
                    half = slice(b * PART, (b + 1) * PART)
                    last = nc.vector.tensor_copy(
                        a_pair[half, s % 2, :].rearrange("p (n t) -> p n t", n=1),
                        a_table[half, bass.ds(chosen[b], 1), :])
                last.then_inc(a_picked, 1)

            def split_v(turn, s):
                if not exists(turn, s):
                    return
                n = turn * RING + s
                past(dve, v_high, n + 1)
                past(dve, out_summed, H * (n - 1))
                nc.vector.scalar_tensor_tensor(out=v_pair[:, s % 2, :], in0=v_hi[:].bitcast(F32),
                                               scalar=low_sb[:, 0:1], in1=ps_v,
                                               op0=ALU.mult, op1=ALU.add).then_inc(v_split, 1)

            def copy_bxt(turn, s):
                if not exists(turn, s):
                    return
                n = turn * RING + s
                past(dve, bx_summed, n + 1)
                past(dve, bx_turned, n)
                nc.vector.tensor_copy(bx_t[:], ps_bx[:, 0:P]).then_inc(bxt_copied, 1)

            def add_tiles(turn, s):
                if not exists(turn, s):
                    return
                n = turn * RING + s
                past(dve, bx_turned, n + 1)
                past(dve, bx_spread, n)
                nc.vector.tensor_reduce(bx_sum[:].rearrange("p b r -> p (b r)"),
                                        ps_s.rearrange("p (g c) -> p c g", c=TILE_COLS),
                                        mybir.AxisListType.X, ALU.add).then_inc(bx_added, 1)

            def step(turn, s, picked):
                split_v(turn, s - 1)
                copy_bxt(turn, s)
                high_x(turn, s + 2)
                add_tiles(turn, s)
                pick_a(turn, s, picked)
                split_w(turn, s + 1)

            dve.wait_ge(w_loaded, PAIR * 16)
            for b in range(PAIR):
                half = slice(b * PART, (b + 1) * PART)
                eye = identity[half, half].rearrange("p (m c) -> p m c", m=1).to_broadcast([PART, mixes, C])
                nc.vector.tensor_tensor(w_full[half], w_full[half], eye, ALU.add).then_inc(w_table, 1)
            for s in range(2):
                high_x(0, s)
            dve.wait_ge(ids_ready, 2)
            for g in range(1, H * K, 2):
                dve.wait_ge(at_spread, g + 1)
                nc.vector.tensor_copy(a_table_part(g), spread_bank(g)).then_inc(at_copied[1], 1)
            dve.wait_ge(consts_loaded, 16)
            split_w(0, 0)
            for half in at_copied:
                dve.wait_ge(half, H * K // 2)
            turns(dve, step)
            split_v(pairs // RING - 1, RING - 1)

        @block.tensor
        def _(pe):
            def keep_clock(times):
                for _ in range(times):
                    nc.tensor.matmul(ps_bx[:], idle_rows[:, 0:P], idle_rows[:], start=True, stop=True)

            pe.wait_ge(idle_ready, 1)
            keep_clock(9)
            pe.wait_ge(identity_loaded, 16)
            pe.wait_ge(a_loaded, 16)
            for h in range(H):
                for n in range(AH):
                    last = nc.tensor.transpose(ps_out[:, 0, h, n * P:(n + 1) * P],
                                               a_rows[:, h * AH + n, :, :].rearrange("p k r -> p (k r)"),
                                               identity[:])
                last.then_inc(at_turned, 1)
            pe.wait_ge(b_loaded, 16)
            for h in range(H):
                for k in range(KH):
                    last = nc.tensor.transpose(ps_xt[:, h, k * P:(k + 1) * P],
                                               b_rows[:, (h * KH + k) * P:(h * KH + k + 1) * P], identity[:])
                last.then_inc(bt_turned, 1)
            pe.wait_ge(bt_copied, H)

            def turn_x(turn, s, h):
                if not exists(turn, s):
                    return
                n = turn * RING + s
                if h == 0:
                    past(pe, x_loaded[s % RING], 16 * (turn + s // RING + 1))
                past(pe, xt_copied, H * (n - 1) + h + 1)
                for k in range(KH):
                    at = (h * KH + k) * P
                    last = nc.tensor.transpose(ps_xt[:, h, k * P:(k + 1) * P],
                                               x_sb[:, s % RING, at:at + P], identity[:])
                last.then_inc(xt_turned, 1)

            def sum_bx(turn, s, h):
                if not exists(turn, s):
                    return
                n = turn * RING + s
                if h == 0:
                    past(pe, b_picked, n + 1)
                    past(pe, bxt_copied, n)
                past(pe, xt_copied, H * n + h + 1)
                for k in range(h * KH, (h + 1) * KH):
                    g = k % 4
                    last = nc.tensor.matmul(ps_bx[g * TILE_COLS:(g + 1) * TILE_COLS, 0:P],
                                            b_pair[:, s % 2, k, :, :].rearrange("p b r -> p (b r)"),
                                            x_t[:, s % 2, k, :], start=(h == 0), stop=(h == H - 1),
                                            tile_position=(0, g * TILE_COLS))
                if h == H - 1:
                    last.then_inc(bx_summed, 1)

            def turn_bx(turn, s):
                if not exists(turn, s):
                    return
                n = turn * RING + s
                past(pe, bxt_copied, n + 1)
                past(pe, bx_added, n)
                past(pe, v_split, n)
                nc.tensor.transpose(ps_s, bx_t[:], identity[:]).then_inc(bx_turned, 1)

            def make_v(turn, s):
                if not exists(turn, s):
                    return
                n = turn * RING + s
                past(pe, bx_spread, n + 1)
                past(pe, w_picked, n + 1)
                for b in range(PAIR):
                    half = slice(b * PART, (b + 1) * PART)
                    last = nc.tensor.matmul(ps_v[half, half], bx[:, half], w_pair[:, s % 2, half],
                                            start=True, stop=True, tile_position=(0, b * PART))
                last.then_inc(v_made, 1)

            def mix(turn, s, h):
                if not exists(turn, s):
                    return
                n = turn * RING + s
                if h == 0:
                    past(pe, w_split, n + 1)
                    past(pe, x_low, n + 1)
                past(pe, y_copied, H * (n - 2) + h + 1)
                cols = slice(h * BANK, (h + 1) * BANK)
                q = s % RING
                hi, lo = w_pair_parts[:, s % 2, 0, :], w_pair_parts[:, s % 2, 1, :]
                nc.tensor.matmul(ps_out[:, s % 2, h, :], hi, x_hi[:, q, cols], start=True, stop=False)
                nc.tensor.matmul(ps_out[:, s % 2, h, :], hi, x_lo[:, q, cols], start=False, stop=False)
                last = nc.tensor.matmul(ps_out[:, s % 2, h, :], lo, x_hi[:, q, cols], start=False, stop=False)
                if h == H - 1:
                    last.then_inc(w_used, 1)

            def add_adapter(turn, s, h):
                if not exists(turn, s):
                    return
                n = turn * RING + s
                if h == 0:
                    past(pe, v_split, n + 1)
                    past(pe, a_picked, n + 1)
                nc.tensor.matmul(ps_out[:, s % 2, h, :], v_pair[:, s % 2, :],
                                 a_pair[:, s % 2, h * BANK:(h + 1) * BANK],
                                 start=False, stop=True).then_inc(out_summed, 1)

            def step(turn, s, _):
                turn_x(turn, s + 1, 0)
                for h in range(H):
                    add_adapter(turn, s - 1, h)
                turn_bx(turn, s)
                mix(turn, s, 0)
                turn_x(turn, s + 1, 1)
                mix(turn, s, 1)
                make_v(turn, s)
                sum_bx(turn, s + 1, 0)
                sum_bx(turn, s + 1, 1)

            def spread_a(steps):
                for g in steps:
                    k, h = g // H, g % H
                    past(pe, at_copied[g % 2], g // 2 - 1)
                    for part in range(2):
                        last = nc.tensor.matmul(spread_bank(g), pick_chunk[:, k, part, :],
                                                a_turned[:, part, h * BANK:(h + 1) * BANK],
                                                start=(part == 0), stop=(part == 1))
                    last.then_inc(at_spread, 1)

            keep_clock(12)
            pe.wait_ge(chunks_ready, K)
            pe.wait_ge(at_low, H)
            spread_a(range(SPREAD_FIRST))
            for h in range(H):
                turn_x(0, 0, h)
            spread_a(range(SPREAD_FIRST, H * K))
            for h in range(H):
                sum_bx(0, 0, h)
            for half in at_copied:
                pe.wait_ge(half, H * K // 2)
            turns(pe, step)
            for h in range(H):
                add_adapter(pairs // RING - 1, RING - 1, h)


_INS = ["x", "itok_B_3_7", "itok_B_0_15", "L0_cond_A", "L0_cond_B", "L1_cond_weights"]


def kernel(**inputs):
    import numpy as _np
    import concourse.bacc as _bacc
    from concourse import mybir as _mybir
    from concourse.bass_utils import run_bass_kernel_spmd as _run

    named = {name: _np.ascontiguousarray(inputs[name]) for name in _INS}
    rank = named["L0_cond_A"].shape[2]
    row = _np.arange(P)
    slot = row // rank % SLOTS
    named["ident"] = _np.eye(P, dtype=_np.float32)
    named["low_rows"] = -(slot // 2)[:, None].astype(_np.float32)
    same_rank = row[:, None] % rank == row[None, :] % rank
    named["slot_part"] = _np.stack([same_rank & (slot[None, :] % 2 == part) for part in range(2)], 1).astype(_np.float32)
    named["chunk_rows"] = _np.repeat(_np.eye(P // rank, dtype=_np.float32), rank, axis=0)

    nc = _bacc.Bacc("TRN2", target_bir_lowering=False, num_devices=1)
    arrays, args = {}, []
    for name, a in named.items():
        arrays[f"in_{name}_dram"] = a
        args.append(nc.dram_tensor(f"in_{name}_dram", a.shape, _mybir.dt.from_np(a.dtype), kind="ExternalInput").ap())
    shape = named["x"].shape
    args.append(nc.dram_tensor("out_0_dram", shape, _mybir.dt.float32, kind="ExternalOutput").ap())
    cond_resid_kernel(nc, *args)
    r = _run(nc, [arrays], core_ids=[0])
    return r.results[0]["out_0_dram"]
```
